# Optimizing a Trainium2 kernel written in Bass

```python
import numpy as np
import jax
import jax.numpy as jnp

def _softmax(x, axis=-1):
    return jax.nn.softmax(x, axis=axis)

def _gelu(x):
    return jax.nn.gelu(x, approximate=True)

def _silu(x):
    return jax.nn.silu(x)

def _sigmoid(x):
    return jax.nn.sigmoid(x)

def _layernorm(x, axis=-1, eps=1e-05):
    m = jnp.mean(x, axis=axis, keepdims=True)
    v = jnp.var(x, axis=axis, keepdims=True)
    return (x - m) / jnp.sqrt(v + eps)

def _scatter_add(tgt, idx, src, axis=0):
    return tgt.at[idx].add(src)

def _segment_sum(src, seg, n):
    return jax.ops.segment_sum(src, seg, n)
kernel_name = 'mk_gnn_resnorm_d4_gnn_r32_ffb62d'

def setup_inputs(seed: int=0):
    np.random.seed(seed)
    _w = jnp.asarray

    def _rec_inputs():
        import jax
        import jax.numpy as jnp
        _gk = jax.random.key(seed)
        x = -0.000202 + 1 * jax.random.normal(jax.random.fold_in(_gk, 1), (3125, 64), jnp.float32)
        _s = jax.random.randint(jax.random.fold_in(_gk, 2), (50000,), 0, 3125, jnp.int32)
        _d = jax.random.randint(jax.random.fold_in(_gk, 3), (50000,), 0, 3125, jnp.int32)
        _loop = jnp.arange(3125, dtype=jnp.int32)
        src = jnp.concatenate([_s, _d, _loop])
        dst = jnp.concatenate([_d, _s, _loop])
        _o = jnp.argsort(dst, stable=True)
        src = src[_o]
        dst = dst[_o]
        edge_type_500 = jax.random.randint(jax.random.fold_in(_gk, 13), (103125,), 0, 500, jnp.int32)
        edge_type_8 = jax.random.randint(jax.random.fold_in(_gk, 14), (103125,), 0, 8, jnp.int32)
        edge_weight = 0.000452788 + 0.999756 * jax.random.normal(jax.random.fold_in(_gk, 15), (103125,), jnp.float32)
        return (x, src, dst, edge_type_500, edge_type_8, edge_weight)
    x, src, dst, edge_type_500, edge_type_8, edge_weight = _rec_inputs()

    def _L0_gnn_setup():
        import jax, jax.numpy as jnp
        import numpy as np
        N_NODES = 3125
        N_EDGES = 50000
        D = 64
        L = 3
        key = jax.random.key(seed)
        ks = jax.random.split(key, 7)
        x = jax.random.normal(ks[0], (N_NODES, D), dtype=jnp.float32)
        edge_index = jax.random.randint(ks[1], (2, N_EDGES), 0, N_NODES, dtype=jnp.int32)
        edge_weights = jax.random.normal(ks[2], (N_EDGES,), dtype=jnp.float32)
        edge_W = jax.random.normal(ks[3], (L, 2 * D + 1, D), dtype=jnp.float32) * 0.1
        edge_b = jnp.zeros((L, D), dtype=jnp.float32)
        node_W = jax.random.normal(ks[4], (L, 2 * D, D), dtype=jnp.float32) * 0.1
        node_b = jnp.zeros((L, D), dtype=jnp.float32)
        return {'x': x, 'edge_index': edge_index, 'edge_weights': edge_weights, 'edge_W': edge_W, 'edge_b': edge_b, 'node_W': node_W, 'node_b': node_b}
    _L0_gnn_all = _L0_gnn_setup()
    _L0_gnn_in = {k: v for k, v in _L0_gnn_all.items() if k in ('edge_W', 'edge_b', 'node_W', 'node_b')}
    del _L0_gnn_all

    def _L1_gnn_setup():
        import jax, jax.numpy as jnp
        import numpy as np
        N_NODES = 50000
        N_EDGES = 25000
        IN_DIM = 64
        OUT_DIM = 64
        NUM_RELS = 8
        key = jax.random.key(seed)
        ks = jax.random.split(key, 9)
        node_features = jax.random.normal(ks[0], (N_NODES, IN_DIM), dtype=jnp.float32)
        src = jax.random.randint(ks[1], (N_EDGES,), 0, N_NODES)
        dst = jax.random.randint(ks[2], (N_EDGES,), 0, N_NODES)
        etypes = jax.random.randint(ks[3], (N_EDGES,), 0, NUM_RELS)
        s_in = 1.0 / np.sqrt(IN_DIM).astype(np.float32)
        s_out = 1.0 / np.sqrt(OUT_DIM).astype(np.float32)
        W_enc = jax.random.normal(ks[4], (IN_DIM, OUT_DIM), dtype=jnp.float32) * s_in
        b_enc = jnp.zeros((OUT_DIM,), dtype=jnp.float32)
        W_rel = jax.random.normal(ks[5], (NUM_RELS, OUT_DIM, OUT_DIM), dtype=jnp.float32) * s_out
        W_self = jax.random.normal(ks[6], (OUT_DIM, OUT_DIM), dtype=jnp.float32) * s_out
        bias = jnp.zeros((OUT_DIM,), dtype=jnp.float32)
        return {'node_features': node_features, 'src': src, 'dst': dst, 'etypes': etypes, 'W_enc': W_enc, 'b_enc': b_enc, 'W_rel': W_rel, 'W_self': W_self, 'bias': bias}
    _L1_gnn_all = _L1_gnn_setup()
    _L1_gnn_in = {k: v for k, v in _L1_gnn_all.items() if k in ('W_enc', 'b_enc', 'W_rel', 'W_self', 'bias')}
    del _L1_gnn_all

    def _L2_gnn_setup():
        import jax, jax.numpy as jnp
        import numpy as np
        N_NODES = 3125
        N_EDGES = 50000
        D_IN = 64
        D_HID = 64
        D_OUT = 64
        key = jax.random.key(seed)
        ks = jax.random.split(key, 8)
        x = jax.random.normal(ks[0], (N_NODES, D_IN), dtype=jnp.float32)
        edge_index = jax.random.randint(ks[1], (2, N_EDGES), 0, N_NODES, dtype=jnp.int64)
        s_in = 1.0 / np.sqrt(D_IN)
        s_hid = 1.0 / np.sqrt(D_HID)
        W1l = jax.random.normal(ks[2], (D_IN, D_HID), dtype=jnp.float32) * s_in
        W1r = jax.random.normal(ks[3], (D_IN, D_HID), dtype=jnp.float32) * s_in
        b1 = jnp.zeros((D_HID,), dtype=jnp.float32)
        W2l = jax.random.normal(ks[4], (D_HID, D_OUT), dtype=jnp.float32) * s_hid
        W2r = jax.random.normal(ks[5], (D_HID, D_OUT), dtype=jnp.float32) * s_hid
        b2 = jnp.zeros((D_OUT,), dtype=jnp.float32)
        return {'x': x, 'edge_index': edge_index, 'W1l': W1l, 'b1': b1, 'W1r': W1r, 'W2l': W2l, 'b2': b2, 'W2r': W2r}
    _L2_gnn_all = _L2_gnn_setup()
    _L2_gnn_in = {k: v for k, v in _L2_gnn_all.items() if k in ('W1l', 'b1', 'W1r', 'W2l', 'b2', 'W2r')}
    del _L2_gnn_all

    def _L3_gnn_setup():
        import jax, jax.numpy as jnp
        import numpy as np
        N_ENT, N_REL, N_EDGE = (50000, 500, 15625)
        L_LAYERS, HEADS, DIM = (2, 2, 64)
        POW_ITER, ALPHA, LN_EPS = (3, 0.15, 1e-05)

        def _layernorm(x, g, b):
            mu = jnp.mean(x, axis=-1, keepdims=True)
            var = jnp.mean(jnp.square(x - mu), axis=-1, keepdims=True)
            return (x - mu) * jax.lax.rsqrt(var + LN_EPS) * g + b

        def _node_scores(h, W, att):
            t = jnp.tanh((h @ W).reshape(h.shape[0], HEADS, DIM))
            return jnp.einsum('mhd,hd->mh', t, att)

        def _segment_softmax(scores, seg, num_segments):
            m = jax.ops.segment_max(scores, seg, num_segments=num_segments)
            e = jnp.exp(scores - m[seg])
            z = jax.ops.segment_sum(e, seg, num_segments=num_segments)
            return e / z[seg]
        key = jax.random.key(seed)
        ks = jax.random.split(key, 13)
        s = 1.0 / np.sqrt(DIM)
        return {'entity_embed': jax.random.normal(ks[0], (N_ENT, DIM), jnp.float32) * 0.05, 'relation_embed': jax.random.normal(ks[1], (N_REL, DIM), jnp.float32) * 0.05, 'edge_index': jax.random.randint(ks[2], (2, N_EDGE), 0, N_ENT, jnp.int32), 'edge_type': jax.random.randint(ks[3], (N_EDGE,), 0, N_REL, jnp.int32), 'ln_gamma': jnp.ones((L_LAYERS, DIM), jnp.float32), 'ln_beta': jnp.zeros((L_LAYERS, DIM), jnp.float32), 'W_h': jax.random.normal(ks[4], (L_LAYERS, DIM, HEADS * DIM), jnp.float32) * s, 'W_t': jax.random.normal(ks[5], (L_LAYERS, DIM, HEADS * DIM), jnp.float32) * s, 'W_r': jax.random.normal(ks[6], (L_LAYERS, DIM, HEADS * DIM), jnp.float32) * s, 'att_h': jax.random.normal(ks[7], (L_LAYERS, HEADS, DIM), jnp.float32) * s, 'att_t': jax.random.normal(ks[8], (L_LAYERS, HEADS, DIM), jnp.float32) * s, 'att_r': jax.random.normal(ks[9], (L_LAYERS, HEADS, DIM), jnp.float32) * s, 'W_o': jax.random.normal(ks[10], (L_LAYERS, HEADS * DIM, DIM), jnp.float32) * s}
    _L3_gnn_all = _L3_gnn_setup()
    _L3_gnn_in = {k: v for k, v in _L3_gnn_all.items() if k in ('relation_embed', 'ln_gamma', 'ln_beta', 'W_h', 'W_t', 'W_r', 'att_h', 'att_t', 'att_r', 'W_o')}
    del _L3_gnn_all
    return {'x': x, 'src': src, 'dst': dst, 'edge_type_500': edge_type_500, 'edge_type_8': edge_type_8, 'edge_weight': edge_weight, 'L0_gnn_edge_W': _L0_gnn_in['edge_W'], 'L0_gnn_edge_b': _L0_gnn_in['edge_b'], 'L0_gnn_node_W': _L0_gnn_in['node_W'], 'L0_gnn_node_b': _L0_gnn_in['node_b'], 'L1_gnn_W_enc': _L1_gnn_in['W_enc'], 'L1_gnn_b_enc': _L1_gnn_in['b_enc'], 'L1_gnn_W_rel': _L1_gnn_in['W_rel'], 'L1_gnn_W_self': _L1_gnn_in['W_self'], 'L1_gnn_bias': _L1_gnn_in['bias'], 'L2_gnn_W1l': _L2_gnn_in['W1l'], 'L2_gnn_b1': _L2_gnn_in['b1'], 'L2_gnn_W1r': _L2_gnn_in['W1r'], 'L2_gnn_W2l': _L2_gnn_in['W2l'], 'L2_gnn_b2': _L2_gnn_in['b2'], 'L2_gnn_W2r': _L2_gnn_in['W2r'], 'L3_gnn_relation_embed': _L3_gnn_in['relation_embed'], 'L3_gnn_ln_gamma': _L3_gnn_in['ln_gamma'], 'L3_gnn_ln_beta': _L3_gnn_in['ln_beta'], 'L3_gnn_W_h': _L3_gnn_in['W_h'], 'L3_gnn_W_t': _L3_gnn_in['W_t'], 'L3_gnn_W_r': _L3_gnn_in['W_r'], 'L3_gnn_att_h': _L3_gnn_in['att_h'], 'L3_gnn_att_t': _L3_gnn_in['att_t'], 'L3_gnn_att_r': _L3_gnn_in['att_r'], 'L3_gnn_W_o': _L3_gnn_in['W_o']}

def reference(x, src, dst, edge_type_500, edge_type_8, edge_weight, L0_gnn_edge_W, L0_gnn_edge_b, L0_gnn_node_W, L0_gnn_node_b, L1_gnn_W_enc, L1_gnn_b_enc, L1_gnn_W_rel, L1_gnn_W_self, L1_gnn_bias, L2_gnn_W1l, L2_gnn_b1, L2_gnn_W1r, L2_gnn_W2l, L2_gnn_b2, L2_gnn_W2r, L3_gnn_relation_embed, L3_gnn_ln_gamma, L3_gnn_ln_beta, L3_gnn_W_h, L3_gnn_W_t, L3_gnn_W_r, L3_gnn_att_h, L3_gnn_att_t, L3_gnn_att_r, L3_gnn_W_o):
    import jax
    import jax.numpy as jnp

    def _L0_gnn_ref(x, edge_index, edge_weights, edge_W, edge_b, node_W, node_b):
        import jax, jax.numpy as jnp
        import numpy as np
        N_NODES = 3125
        N_EDGES = 50000
        D = 64
        L = 3
        src, dst = (edge_index[0], edge_index[1])
        ew = edge_weights[:, None]
        n = x.shape[0]
        for l in range(edge_W.shape[0]):
            m = jnp.concatenate([x[src], x[dst], ew], axis=-1)
            m = jax.nn.relu(m @ edge_W[l] + edge_b[l])
            agg = jax.ops.segment_sum(m, dst, num_segments=n)
            x = jax.nn.relu(jnp.concatenate([x, agg], axis=-1) @ node_W[l] + node_b[l])
        return x

    def _L1_gnn_ref(node_features, src, dst, etypes, W_enc, b_enc, W_rel, W_self, bias):
        import jax, jax.numpy as jnp
        import numpy as np
        N_NODES = 50000
        N_EDGES = 25000
        IN_DIM = 64
        OUT_DIM = 64
        NUM_RELS = 8
        n_nodes = node_features.shape[0]
        h0 = jax.nn.relu(node_features @ W_enc + b_enc)
        hW = jnp.einsum('nd,rdo->rno', h0, W_rel)
        msgs = hW[etypes, src]
        agg = jax.ops.segment_sum(msgs, dst, num_segments=n_nodes)
        h1 = jax.nn.relu(agg + h0 @ W_self + bias)
        return h0 + h1

    def _L2_gnn_ref(x, edge_index, W1l, b1, W1r, W2l, b2, W2r):
        import jax, jax.numpy as jnp
        import numpy as np
        N_NODES = 3125
        N_EDGES = 50000
        D_IN = 64
        D_HID = 64
        D_OUT = 64
        n = x.shape[0]
        src, dst = (edge_index[0], edge_index[1])
        deg = jax.ops.segment_sum(jnp.ones(src.shape[0], x.dtype), dst, num_segments=n)
        inv_deg = 1.0 / jnp.maximum(deg, 1.0)

        def sage(h, Wl, b, Wr):
            agg = jax.ops.segment_sum(h[src], dst, num_segments=n) * inv_deg[:, None]
            return agg @ Wl + b + h @ Wr
        h = jax.nn.relu(sage(x, W1l, b1, W1r))
        out = jax.nn.relu(sage(h, W2l, b2, W2r))
        return out

    def _L3_gnn_ref(entity_embed, relation_embed, edge_index, edge_type, ln_gamma, ln_beta, W_h, W_t, W_r, att_h, att_t, att_r, W_o):
        import jax, jax.numpy as jnp
        import numpy as np
        N_ENT, N_REL, N_EDGE = (50000, 500, 15625)
        L_LAYERS, HEADS, DIM = (2, 2, 64)
        POW_ITER, ALPHA, LN_EPS = (3, 0.15, 1e-05)

        def _layernorm(x, g, b):
            mu = jnp.mean(x, axis=-1, keepdims=True)
            var = jnp.mean(jnp.square(x - mu), axis=-1, keepdims=True)
            return (x - mu) * jax.lax.rsqrt(var + LN_EPS) * g + b

        def _node_scores(h, W, att):
            t = jnp.tanh((h @ W).reshape(h.shape[0], HEADS, DIM))
            return jnp.einsum('mhd,hd->mh', t, att)

        def _segment_softmax(scores, seg, num_segments):
            m = jax.ops.segment_max(scores, seg, num_segments=num_segments)
            e = jnp.exp(scores - m[seg])
            z = jax.ops.segment_sum(e, seg, num_segments=num_segments)
            return e / z[seg]
        src, dst = (edge_index[0], edge_index[1])
        n = entity_embed.shape[0]
        ent = entity_embed
        for l in range(L_LAYERS):
            x = ent
            h = _layernorm(x, ln_gamma[l], ln_beta[l])
            s_h = _node_scores(h, W_h[l], att_h[l])
            s_t = _node_scores(h, W_t[l], att_t[l])
            s_r = _node_scores(relation_embed, W_r[l], att_r[l])
            scores = jax.nn.leaky_relu(s_h[src] + s_t[dst] + s_r[edge_type])
            w = _segment_softmax(scores, src, n)
            A = (1.0 - ALPHA) * w
            Z = jnp.broadcast_to(h[:, None, :], (n, HEADS, DIM))
            aZ0 = ALPHA * h[:, None, :]
            for _ in range(POW_ITER):
                msg = A[:, :, None] * Z[dst]
                Z = jax.ops.segment_sum(msg, src, num_segments=n) + aZ0
            conv = Z.reshape(n, HEADS * DIM) @ W_o[l]
            ent = conv + x
        return ent
    edge_index = jnp.stack([src, dst])
    x = _layernorm(x + _L0_gnn_ref(x, edge_index, edge_weight, L0_gnn_edge_W, L0_gnn_edge_b, L0_gnn_node_W, L0_gnn_node_b), axis=-1)
    x = _layernorm(x + _L1_gnn_ref(x, src, dst, edge_type_8, L1_gnn_W_enc, L1_gnn_b_enc, L1_gnn_W_rel, L1_gnn_W_self, L1_gnn_bias), axis=-1)
    x = _layernorm(x + _L2_gnn_ref(x, edge_index, L2_gnn_W1l, L2_gnn_b1, L2_gnn_W1r, L2_gnn_W2l, L2_gnn_b2, L2_gnn_W2r), axis=-1)
    x = _layernorm(x + _L3_gnn_ref(x, L3_gnn_relation_embed, edge_index, edge_type_500, L3_gnn_ln_gamma, L3_gnn_ln_beta, L3_gnn_W_h, L3_gnn_W_t, L3_gnn_W_r, L3_gnn_att_h, L3_gnn_att_t, L3_gnn_att_r, L3_gnn_W_o), axis=-1)
    return x

_drawn_inputs = setup_inputs


def setup_inputs(seed=0):
    import zlib

    import numpy as np

    out = dict(_drawn_inputs(seed))
    spreads = {'L0_gnn_edge_b': (0.0, 0.1),
     'L0_gnn_node_b': (0.0, 0.8),
     'L1_gnn_b_enc': (0.0, 0.1),
     'L1_gnn_bias': (0.0, 0.433),
     'L2_gnn_b1': (0.0, 0.1),
     'L2_gnn_b2': (0.0, 0.1),
     'L3_gnn_ln_gamma': (1.0, 0.2),
     'L3_gnn_ln_beta': (0.0, 0.1)}
    factors = {'edge_weight': 8.0,
     'L3_gnn_relation_embed': 8.0,
     'L3_gnn_W_h': 8.0,
     'L3_gnn_W_t': 3.172,
     'L3_gnn_W_r': 8.0,
     'L3_gnn_att_h': 8.0,
     'L3_gnn_att_t': 3.897,
     'L3_gnn_att_r': 8.0}
    for name, (base, spread) in spreads.items():
        noise = np.random.default_rng([zlib.crc32(name.encode()), seed]).standard_normal(out[name].shape)
        drawn = base * np.exp(spread * noise) if base else spread * noise
        out[name] = jnp.asarray(drawn.astype(out[name].dtype))
    for name, factor in factors.items():
        out[name] = (out[name] * factor).astype(out[name].dtype)
    return out
```

```python
import numpy as np
import concourse.bass as bass
from concourse import mybir
from contextlib import ExitStack

FP32, BF16, FP16 = mybir.dt.float32, mybir.dt.bfloat16, mybir.dt.float16
I32, I16, U32 = mybir.dt.int32, mybir.dt.int16, mybir.dt.uint32
ALU = mybir.AluOpType
ACT = mybir.ActivationFunctionType
AX = mybir.AxisListType
ds = bass.ds

P = 128
D = 64
NODES = 3125
EDGES = 103125
BLK = -(-NODES // P)
LAST = BLK - 1
ROWS = -(-EDGES // P)
RTILES = -(-ROWS // P)
TAIL = EDGES - (ROWS - 1) * P
GRP = 13
STEPS = ROWS // GRP
QUARTERS = 361
CHUNKS = 4 * QUARTERS
assert CHUNKS >= (EDGES + BLK * BLK * (P - 1)) // P and GRP * STEPS == ROWS
KT = -(-CHUNKS // P)
NONE = 255
BIG = 3.0e38
REC = 8
CTL = 16
RELS, RELS_BIG, HEADS, LAYERS = 8, 500, 2, 2
RB = -(-RELS_BIG // P)


class Counted:

    def __init__(self, handle):
        self.h, self.at = handle, 0


def after(eng, sem, value, apart=False):
    if not isinstance(value, int):
        eng.wait_ge(sem.h, value)
        if apart or eng.engine == mybir.EngineType.Pool:
            eng.nop(nofuse=True)
    elif value > 0:
        eng.wait_ge(sem.h, value)


class Program:
    def __init__(self, nc, ctx, ins, out):
        self.nc, self.ctx, self.ins, self.out = nc, ctx, ins, out
        self.sems = {}
        self.names = {}

    def sb(self, name, shape, dt, ctx=None):
        self.names[name] = n = self.names.get(name, 0) + 1
        return (ctx or self.ctx).enter_context(self.nc.sbuf_tensor(f"{name}_{n}", shape, dt))

    def ps(self, name, shape, ctx, dt=FP32):
        self.names[name] = n = self.names.get(name, 0) + 1
        return ctx.enter_context(self.nc.psum_tensor(f"{name}_{n}", shape, dt))

    def dram(self, name, shape, dt):
        return self.nc.dram_tensor(name, shape, dt).ap()

    def sem(self, name):
        if name not in self.sems:
            self.sems[name] = Counted(self.ctx.enter_context(self.nc.semaphore(name)))
        return self.sems[name]

    def block(self):
        return self.nc.Block()


def chain(eng, sem, ops):
    for op in ops:
        op().then_inc(sem.h, 1)
        sem.at += 1
        eng.wait_ge(sem.h, sem.at)


def constants(p):
    nc = p.nc
    p.row = p.sb("iota_row", [P, P], FP32)
    p.row16 = p.sb("iota_row16", [P, P], FP16)
    p.col = p.sb("iota_col", [P, 8], FP32)
    p.ident = p.sb("ident", [P, P], FP32)
    p.below = p.sb("below", [P, P], FP16)
    p.upper = p.sb("upper", [P, P], FP32)
    p.ones = p.sb("ones", [P, P], FP32)
    p.onesb = p.sb("onesb", [P, 2], BF16)
    made, ready = p.sem("iotas"), p.sem("dve")
    with p.block() as block:
        @block.gpsimd
        def _(eng):
            eng.iota(p.row[:], [[1, P]], base=0, channel_multiplier=0,
                     allow_small_or_imprecise_dtypes=True).then_inc(made.h, 1)
            eng.iota(p.col[:], [[P, 8]], base=0, channel_multiplier=1,
                     allow_small_or_imprecise_dtypes=True).then_inc(made.h, 1)
            made.at += 2

        @block.vector
        def _(eng):
            eng.wait_ge(made.h, 2)
            c0 = p.col[:, 0:1]
            for op in (
                lambda: eng.tensor_scalar(p.ident[:], p.row[:], c0, None, ALU.is_equal),
                lambda: eng.tensor_scalar(p.below[:], p.row[:], c0, None, ALU.is_lt),
                lambda: eng.tensor_scalar(p.upper[:], p.row[:], c0, None, ALU.is_gt),
                lambda: eng.tensor_copy(p.row16[:], p.row[:]),
                lambda: eng.memset(p.ones[:], 1.0),
                lambda: eng.memset(p.onesb[:], 1.0),
            ):
                op().then_inc(ready.h, 1)
                ready.at += 1


def load_edges(p, s):
    nc, ins = p.nc, p.ins
    ctx = ExitStack()
    with ctx:
        raw = p.sb("raw", [P, 4, RTILES, P], I32, ctx)
        part = p.sb("part", [P, 6, RTILES, P], I32, ctx)
        frow = p.sb("frow", [P, 7, RTILES, P], FP32, ctx)
        keyf = p.sb("keyf", [P, RTILES, P], FP32, ctx)
        rows16 = p.sb("rows16", [P, 3, RTILES, P], FP16, ctx)
        turned = p.ps("turned", [P, 2, 512], ctx)
        loaded, v, turn, got, filled = (p.sem(x) for x in ("loaded", "dve", "pe", "act", "pool"))
        l0, v0, t0, g0, f0 = loaded.at, v.at, turn.at, got.at, filled.at
        srcs = [ins["src"], ins["dst"], ins["edge_type_8"], ins["edge_type_500"]]
        full = RTILES - 1
        last = ROWS - 1 - full * P
        with p.block() as block:
            @block.gpsimd
            def _(eng):
                eng.memset(raw[:, 0:2, full, :], 31 * P).then_inc(filled.h, 1)
                eng.memset(raw[:, 2:4, full, :], 0).then_inc(filled.h, 1)
                eng.memset(frow[:, 3, full, :], 0.0).then_inc(filled.h, 1)
                filled.at += 3

            @block.sync
            def _(eng):
                eng.wait_ge(filled.h, f0 + 3)
                for i, a in enumerate(srcs + [ins["edge_weight"]]):
                    to = raw[:, i] if i < 4 else frow[:, 3]
                    eng.dma_start(to[:, 0:full, :], a[0:full * P * P].rearrange(
                        "(j p e) -> p j e", p=P, e=P)).then_inc(loaded.h, 16)
                    eng.dma_start(to[0:last, full, :], a[full * P * P:(ROWS - 1) * P].rearrange(
                        "(p e) -> p e", e=P)).then_inc(loaded.h, 16)
                    eng.dma_start(to[last:last + 1, full, 0:TAIL],
                                  a[(ROWS - 1) * P:EDGES].unsqueeze(0)).then_inc(loaded.h, 16)
                    loaded.at += 48
                eng.wait_ge(v.h, v0 + 14)
                for i, to in enumerate((s.key_rows, s.sblk_rows, s.type_rows)):
                    eng.dma_start(to.rearrange("(j p e) -> p j e", p=P, e=P),
                                  rows16[:, i]).then_inc(loaded.h, 16)
                    loaded.at += 16
                eng.wait_ge(loaded.h, loaded.at)

            @block.vector
            def _(eng):
                eng.wait_ge(loaded.h, l0 + 240)
                def do(op):
                    op.then_inc(v.h, 1)
                    v.at += 1
                for i in range(2):
                    do(eng.tensor_scalar(part[:, 2 * i], raw[:, i], P - 1, None, ALU.bitwise_and))
                    do(eng.tensor_scalar(part[:, 2 * i + 1], raw[:, i], 7, None,
                                         ALU.logical_shift_right))
                eng.wait_ge(v.h, v0 + 4)
                do(eng.tensor_copy(frow[:, 0], part[:, 0]))
                do(eng.tensor_copy(frow[:, 1], part[:, 2]))
                do(eng.tensor_copy(frow[:, 2], raw[:, 2]))
                do(eng.tensor_copy(frow[:, 4], part[:, 1]))
                do(eng.tensor_copy(frow[:, 5], part[:, 3]))
                do(eng.tensor_copy(frow[:, 6], raw[:, 3]))
                eng.wait_ge(v.h, v0 + 10)
                do(eng.scalar_tensor_tensor(keyf[:], frow[:, 4], 32.0, frow[:, 5], ALU.mult, ALU.add))
                eng.wait_ge(v.h, v0 + 11)
                do(eng.tensor_copy(rows16[:, 0], keyf[:]))
                do(eng.tensor_copy(rows16[:, 1], frow[:, 4]))
                do(eng.tensor_copy(rows16[:, 2], frow[:, 6]))

            @block.tensor
            def _(eng):
                eng.wait_ge(v.h, v0 + 10)
                for i in range(7):
                    for j in range(RTILES):
                        n = i * RTILES + j
                        k = min(P, ROWS - j * P)
                        after(eng, got, g0 + n - 1 if n >= 2 else 0)
                        eng.transpose(turned[:, n % 2, 0:k], frow[0:k, i, j, :],
                                      p.ident[0:k, 0:k]).then_inc(turn.h, 1)
                        turn.at += 1

            @block.scalar
            def _(eng):
                for i in range(7):
                    for j in range(RTILES):
                        n = i * RTILES + j
                        k = min(P, ROWS - j * P)
                        to = (s.rec[:, j * P:j * P + k, i] if i < 4
                              else s.edge_cols[:, i - 4, j * P:j * P + k])
                        eng.wait_ge(turn.h, t0 + n + 1)
                        eng.copy(to, turned[:, n % 2, 0:k]).then_inc(got.h, 1)
                        got.at += 1


def one_hot_columns(eng, out, cols, p):
    return eng.tensor_tensor(out, cols.unsqueeze(2).to_broadcast([P, GRP, BLK]),
                             p.row[:, 0:BLK].unsqueeze(1).to_broadcast([P, GRP, BLK]),
                             ALU.is_equal)


def count_buckets(p, s):
    nc = p.nc
    ctx = ExitStack()
    with ctx:
        so = p.sb("so", [P, 2, GRP, BLK], BF16, ctx)
        do_ = p.sb("do", [P, 2, GRP, BLK], BF16, ctx)
        counts = [p.ps("counts", [P, 512], ctx) for _ in range(2)]
        v, pe, act = p.sem("dve"), p.sem("pe"), p.sem("act")
        v0, p0, a0 = v.at, pe.at, act.at
        with p.block() as block:
            @block.vector
            def _(eng):
                eng.memset(s.before[:, 0, :], 0.0)
                def step(g, h):
                    after(eng, pe, p0 + g - 1 if not (isinstance(g, int) and g < 2) else 0)
                    one_hot_columns(eng, so[:, h], s.edge_cols[:, 0, ds(g * GRP, GRP)], p).then_inc(v.h, 1)
                    one_hot_columns(eng, do_[:, h], s.edge_cols[:, 1, ds(g * GRP, GRP)], p).then_inc(v.h, 1)
                step(0, 0)
                step(1, 1)
                with eng.Fori(1, STEPS // 2) as i:
                    step(i * 2, 0)
                    step(i * 2 + 1, 1)
                v.at += 2 * STEPS
                eng.wait_ge(act.h, a0 + STEPS)
                for b in range(BLK):
                    h = s.before[:, 1:ROWS + 1, b]
                    eng.tensor_tensor_scan(h, s.ones_row[:], h, 0.0, ALU.mult, ALU.add).then_inc(v.h, 1)
                    v.at += 1
                eng.wait_ge(v.h, v.at)

            @block.tensor
            def _(eng):
                def step(g, h):
                    after(eng, v, v0 + 2 * g + 2)
                    after(eng, act, a0 + g - 1 if not (isinstance(g, int) and g < 2) else 0)
                    for c in range(GRP):
                        mm = eng.matmul(counts[h][0:BLK, c * BLK:(c + 1) * BLK], so[:, h, c, :],
                                        do_[:, h, c, :], start=True, stop=True)
                    mm.then_inc(pe.h, 1)
                step(0, 0)
                step(1, 1)
                with eng.Fori(1, STEPS // 2) as i:
                    step(i * 2, 0)
                    step(i * 2 + 1, 1)
                pe.at += STEPS

            @block.scalar
            def _(eng):
                def step(g, h):
                    after(eng, pe, p0 + g + 1)
                    eng.copy(s.before[:, ds(g * GRP + 1, GRP), :],
                             counts[h][0:BLK, 0:GRP * BLK].rearrange("p (c b) -> p c b", b=BLK)
                             ).then_inc(act.h, 1)
                with eng.Fori(0, STEPS // 2) as i:
                    step(i * 2, 0)
                    step(i * 2 + 1, 1)
                act.at += STEPS


def place_buckets(p, s):
    nc = p.nc
    ctx = ExitStack()
    with ctx:
        tot = p.sb("tot", [BLK, BLK], FP32, ctx)
        toti = p.sb("toti", [BLK, 2, BLK], I32, ctx)
        nch = p.sb("nch", [BLK, BLK], FP32, ctx)
        end = p.sb("end", [BLK, BLK], FP32, ctx)
        start = p.sb("start", [BLK, BLK], FP32, ctx)
        rowpre = p.sb("rowpre", [BLK, 1], FP32, ctx)
        ends = p.sb("ends", [P, BLK * BLK], FP32, ctx)
        junk = p.sb("junk", [P, BLK * BLK], FP32, ctx)
        kcol = p.sb("kcol", [P, KT], FP32, ctx)
        bkt = p.sb("bkt", [P, 2, KT], FP32, ctx)
        bs = p.sb("bs", [P, 2, KT], FP32, ctx)
        bT = p.sb("bT", [KT, 2, P], FP32, ctx)
        ps = p.ps("prefix", [P, 512], ctx)
        v, pe, ld, pool = p.sem("dve"), p.sem("pe"), p.sem("loaded"), p.sem("pool")
        v0, p0, l0, q0 = v.at, pe.at, ld.at, pool.at
        with p.block() as block:
            @block.gpsimd
            def _(eng):
                eng.iota(kcol[:], [[P, KT]], base=0, channel_multiplier=1,
                         allow_small_or_imprecise_dtypes=True).then_inc(pool.h, 1)
                pool.at += 1

            @block.vector
            def _(eng):
                chain(eng, v, [
                    lambda: eng.tensor_scalar(tot[:], s.before[:, ROWS, :], float(P - 1), None, ALU.add),
                    lambda: eng.tensor_copy(toti[:, 0], tot[:]),
                    lambda: eng.tensor_scalar(toti[:, 1], toti[:, 0], 7, None, ALU.logical_shift_right),
                    lambda: eng.tensor_copy(nch[:], toti[:, 1]),
                    lambda: eng.tensor_tensor_scan(end[:], p.ones[0:BLK, 0:BLK], nch[:], 0.0,
                                                   ALU.mult, ALU.add)])
                s.p_a = v.at
                eng.wait_ge(pe.h, p0 + 1)
                chain(eng, v, [
                    lambda: eng.tensor_copy(rowpre[:], ps[0:BLK, 0:1]),
                    lambda: eng.tensor_scalar(end[:], end[:], rowpre[:], None, ALU.add)])
                s.p_b = v.at
                chain(eng, v, [
                    lambda: eng.tensor_tensor(start[:], end[:], nch[:], ALU.subtract),
                    lambda: eng.tensor_scalar(start[:], start[:], float(P), None, ALU.mult),
                    lambda: eng.tensor_tensor(s.before[:], s.before[:],
                                              start[:].unsqueeze(1).to_broadcast([BLK, ROWS + 1, BLK]),
                                              ALU.add)])
                eng.wait_ge(ld.h, l0 + 32)
                eng.wait_ge(pool.h, q0 + 1)
                for j in range(KT):
                    chain(eng, v, [
                        lambda: eng.tensor_scalar(junk[:], ends[:], kcol[:, j:j + 1], None, ALU.is_le,
                                                  ALU.add, accum_out=bs[:, 1, j:j + 1]),
                        lambda: eng.tensor_scalar(junk[:, 0:BLK], ends[:, BLK - 1:BLK * BLK:BLK],
                                                  kcol[:, j:j + 1], None, ALU.is_le,
                                                  ALU.add, accum_out=bs[:, 0, j:j + 1])])
                chain(eng, v, [
                    lambda: eng.tensor_scalar(bkt[:, 0], bs[:, 0], float(BLK - 1), None, ALU.min),
                    lambda: eng.tensor_scalar(bkt[:, 1], bs[:, 1], float(BLK * BLK - 1), None, ALU.min),
                    lambda: eng.scalar_tensor_tensor(bkt[:, 1], bkt[:, 0], -float(BLK), bkt[:, 1],
                                                     ALU.mult, ALU.add)])
                s.p_c = v.at
                eng.wait_ge(pe.h, p0 + 3)
                for i in range(2):
                    chain(eng, v, [lambda: eng.tensor_copy(bT[:, i], ps[0:KT, P * (i + 1):P * (i + 2)])])
                s.p_d = v.at

            @block.tensor
            def _(eng):
                eng.wait_ge(v.h, s.p_a)
                eng.matmul(ps[0:BLK, 0:1], p.upper[0:BLK, 0:BLK], end[:, BLK - 1:BLK],
                           start=True, stop=True).then_inc(pe.h, 1)
                eng.wait_ge(v.h, s.p_c)
                for i in range(2):
                    eng.transpose(ps[0:KT, P * (i + 1):P * (i + 2)], bkt[:, i], p.ident[:]).then_inc(pe.h, 1)
                pe.at += 3

            @block.sync
            def _(eng):
                eng.wait_ge(v.h, s.p_b)
                eng.dma_start(s.ends_d.rearrange("(a b) -> a b", b=BLK), end[:]).then_inc(ld.h, 16)
                eng.wait_ge(ld.h, l0 + 16)
                eng.dma_start(ends[:], s.ends_d.partition_broadcast(P)).then_inc(ld.h, 16)
                eng.wait_ge(v.h, s.p_d)
                for i in range(2):
                    eng.dma_start(s.blocks_d[i].rearrange("(j e) -> j e", e=P), bT[:, i]).then_inc(ld.h, 16)
                eng.wait_ge(ld.h, l0 + 64)
                ld.at += 64


def relation_scores(p, s):
    nc, ins = p.nc, p.ins
    ctx = ExitStack()
    W = HEADS * D
    with ctx:
        rel = p.sb("rel", [P, RB, P], FP32, ctx)
        relT = p.sb("relT", [P, RB, P], FP32, ctx)
        wr = p.sb("wr", [D, LAYERS, W], FP32, ctx)
        att = p.sb("att", [P, LAYERS, W], FP32, ctx)
        th = p.sb("th", [P, RB, LAYERS, W], FP32, ctx)
        sc = p.sb("sc", [P, RB, LAYERS, HEADS], FP32, ctx)
        ps = p.ps("relp", [P, 512], ctx)
        po = p.ps("relo", [P, RB, 512], ctx)
        v, pe, ld, act = p.sem("dve"), p.sem("pe"), p.sem("loaded"), p.sem("act")
        v0, p0, l0, a0 = v.at, pe.at, ld.at, act.at
        last = RELS_BIG - (RB - 1) * P
        with p.block() as block:
            @block.sync
            def _(eng):
                r = ins["L3_gnn_relation_embed"]
                eng.wait_ge(v.h, v0 + 1)
                eng.dma_start(rel[:, 0:RB - 1, 0:D], r[0:(RB - 1) * P, :].rearrange(
                    "(j p) f -> p j f", p=P)).then_inc(ld.h, 16)
                eng.dma_start(rel[0:last, RB - 1, 0:D], r[(RB - 1) * P:RELS_BIG, :]).then_inc(ld.h, 16)
                eng.dma_start(wr[:], ins["L3_gnn_W_r"].rearrange("l d w -> d l w")).then_inc(ld.h, 16)
                eng.dma_start(att[:], ins["L3_gnn_att_r"].rearrange("l h d -> (l h d)")
                              .partition_broadcast(P)).then_inc(ld.h, 16)
                eng.wait_ge(ld.h, l0 + 64)
                ld.at += 64

            @block.tensor
            def _(eng):
                eng.wait_ge(ld.h, l0 + 64)
                for j in range(RB):
                    mm = eng.transpose(ps[:, j * P:(j + 1) * P], rel[:, j, :], p.ident[:])
                mm.then_inc(pe.h, 1)
                eng.wait_ge(v.h, v0 + 2)
                for j in range(RB):
                    for l in range(LAYERS):
                        mm = eng.matmul(po[:, j, l * W:(l + 1) * W], relT[0:D, j, :], wr[:, l, :],
                                        start=True, stop=True)
                mm.then_inc(pe.h, 1)
                pe.at += 2

            @block.scalar
            def _(eng):
                eng.wait_ge(pe.h, p0 + 2)
                for j in range(RB):
                    eng.activation(th[:, j], po[:, j, 0:LAYERS * W].rearrange("p (l w) -> p l w", w=W),
                                   ACT.Tanh).then_inc(act.h, 1)
                    act.at += 1

            @block.vector
            def _(eng):
                chain(eng, v, [lambda: eng.memset(rel[:], 0.0)])
                eng.wait_ge(pe.h, p0 + 1)
                chain(eng, v, [lambda: eng.tensor_copy(relT[:], ps[:].rearrange("p (j r) -> p j r", r=P))])
                eng.wait_ge(act.h, a0 + RB)
                eng.wait_ge(ld.h, l0 + 64)
                chain(eng, v, [
                    lambda: eng.tensor_tensor(th[:], th[:], att[:].unsqueeze(1).to_broadcast(
                        [P, RB, LAYERS, W]), ALU.mult),
                    lambda: eng.tensor_reduce(sc[:].rearrange("p j l h -> p (j l h)"),
                                              th[:].rearrange("p j l (h d) -> p (j l h) d", d=D),
                                              AX.X, ALU.add)])
                split(eng, v, sc[:].rearrange("p j l h -> p j (l h)"),
                      [s.rel_parts[:, :, i, :] for i in range(3)])


def split(eng, v, x, parts):
    chain(eng, v, [
        lambda: eng.tensor_copy(parts[0], x),
        lambda: eng.tensor_tensor(x, x, parts[0], ALU.subtract),
        lambda: eng.tensor_copy(parts[1], x),
        lambda: eng.tensor_tensor(parts[2], x, parts[1], ALU.subtract)])


def sort_edges(p, s):
    nc = p.nc
    ctx = ExitStack()
    GE = GRP * P
    with ctx:
        key_b = p.sb("key_b", [P, 2, GE], FP16, ctx)
        sb_b = p.sb("sb_b", [BLK, 2, GE], FP16, ctx)
        ty_b = p.sb("ty_b", [P, 2, GE], FP16, ctx)
        key_c = p.sb("key_c", [P, ROWS], FP32, ctx)
        soT = p.sb("soT", [BLK, 2, GE], FP32, ctx)
        dox = p.sb("dox", [P, 2, GRP, BLK], FP32, ctx)
        tyT = p.sb("tyT", [P, 2, RB, GE], BF16, ctx)
        junk = p.sb("junkr", [P, GRP, P], FP16, ctx)
        rank = p.sb("rank", [P, 2, GRP], FP32, ctx)
        picked = p.sb("picked", [P, GRP, BLK], FP32, ctx)
        pos = p.sb("pos", [P, GRP], FP32, ctx)
        posi = p.sb("posi", [P, 3, GRP], I32, ctx)
        posf = p.sb("posf", [P, 2, GRP], FP32, ctx)
        place = p.sb("place", [P, 2, GRP], I32, ctx)
        recs = p.sb("recs", [P, 2, GRP, REC], FP32, ctx)
        spare = p.sb("spare", [P, 1], FP32, ctx)
        real = p.sb("real", [P, ROWS], FP32, ctx)
        aside = p.sb("aside", [P, ROWS], FP32, ctx)
        base = [p.ps("base", [P, 512], ctx) for _ in range(2)]
        relg = [p.ps("relg", [P, 512], ctx) for _ in range(2)]
        v, pe, pool = p.sem("dve"), p.sem("pe"), p.sem("pool")
        rows = [p.sem("rows_a"), p.sem("rows_b")]
        hot, lookd, ready = p.sem("sort_hot"), p.sem("sort_found"), p.sem("sort_ready")
        sent = [p.sem("sent_a"), p.sem("sent_b")]
        init = p.sem("loaded")
        i0 = init.at
        L, S = p.sem("dve_sort"), STEPS
        with p.block() as block:
            def body(eng, step):
                step(0, 0, True)
                step(1, 1, True)
                with eng.Fori(1, S // 2) as i:
                    step(i * 2, 0, False)
                    step(i * 2 + 1, 1, False)

            @block.sync
            def _(eng):
                at = s.sorted_d[0:P * CHUNKS, :].rearrange("(p q k) r -> q p (k r)", p=P, q=4)
                for q in range(4):
                    eng.dma_start(at[q], s.empty[:].rearrange("p k r -> p (k r)")).then_inc(init.h, 16)
                eng.wait_ge(init.h, i0 + 64)
                init.at += 64
                def step(g, h, first):
                    if not first:
                        after(eng, hot, g - 1)
                    at = ds(g * GE, GE)
                    eng.dma_start(key_b[:, h], s.key_rows[at].partition_broadcast(P)).then_inc(rows[h].h, 16)
                    eng.dma_start(sb_b[:, h], s.sblk_rows[at].partition_broadcast(BLK)).then_inc(rows[h].h, 16)
                    eng.dma_start(ty_b[:, h], s.type_rows[at].partition_broadcast(P)).then_inc(rows[h].h, 16)
                body(eng, step)

            @block.vector
            def _(eng):
                chain(eng, v, [
                    lambda: eng.scalar_tensor_tensor(key_c[:], s.edge_cols[:, 0, :], 32.0,
                                                     s.edge_cols[:, 1, :], ALU.mult, ALU.add),
                    lambda: eng.tensor_scalar(spare[:], p.col[:, 0:1], float(P * CHUNKS), None, ALU.add),
                    lambda: eng.tensor_scalar(real[:], s.edge_cols[:, 0, :], float(BLK), None, ALU.is_lt),
                    lambda: eng.tensor_scalar(aside[:], s.edge_cols[:, 0, :], float(BLK), spare[:],
                                              ALU.is_ge, ALU.mult)])
                n = 11
                def step(g, h, first):
                    after(eng, rows[h], 48 * ((g - h) // 2 + 1) if first else 24 * (g - h) + 48)
                    if not first:
                        after(eng, lookd, g - 1)
                    eng.tensor_scalar(soT[:, h], sb_b[:, h], p.col[0:BLK, 0:1], None, ALU.is_equal)
                    for t in range(RB):
                        eng.tensor_scalar(tyT[:, h, t], ty_b[:, h], p.col[:, t:t + 1], None, ALU.is_equal)
                    for c in range(GRP):
                        eng.scalar_tensor_tensor(junk[:, c], key_b[:, h, c * P:(c + 1) * P],
                                                 key_c[:, ds(g * GRP + c, 1)], p.below[:],
                                                 ALU.is_equal, ALU.mult, accum_out=rank[:, h, c:c + 1])
                    one_hot_columns(eng, dox[:, h], s.edge_cols[:, 1, ds(g * GRP, GRP)], p).then_inc(hot.h, 1)
                    after(eng, lookd, g + 1)
                    after(eng, hot, g + 1)
                    if not first:
                        after(eng, sent[h], (g - h) * (8 * GRP))
                    d = lambda op, k: (op.then_inc(L.h, 1), eng.wait_ge(L.h, g * n + k))
                    d(eng.tensor_tensor(picked[:], base[h][:, 0:GRP * BLK].rearrange("p (c b) -> p c b", b=BLK),
                                        dox[:, h], ALU.mult), 1)
                    d(eng.tensor_reduce(pos[:], picked[:], AX.X, ALU.add), 2)
                    d(eng.tensor_tensor(pos[:], pos[:], rank[:, h], ALU.add), 3)
                    d(eng.tensor_copy(posi[:, 0], pos[:]), 4)
                    d(eng.tensor_scalar(posi[:, 1], posi[:, 0], P - 1, None, ALU.bitwise_and), 5)
                    d(eng.tensor_scalar(posi[:, 2], posi[:, 0], 7, None, ALU.logical_shift_right), 6)
                    d(eng.tensor_copy(posf[:], posi[:, 1:3]), 7)
                    d(eng.scalar_tensor_tensor(pos[:], posf[:, 0], float(CHUNKS), posf[:, 1],
                                               ALU.mult, ALU.add), 8)
                    d(eng.tensor_tensor(pos[:], pos[:], real[:, ds(g * GRP, GRP)], ALU.mult), 9)
                    d(eng.tensor_tensor(pos[:], pos[:], aside[:, ds(g * GRP, GRP)], ALU.add), 10)
                    d(eng.tensor_copy(place[:, h], pos[:]), 11)
                    eng.tensor_copy(recs[:, h, :, 0:4], s.rec[:, ds(g * GRP, GRP), :])
                    eng.tensor_reduce(recs[:, h, :, 4:8],
                                      relg[h][:, 0:GRP * 12].rearrange("p (c i r) -> p c r i", i=3, r=4),
                                      AX.X, ALU.add).then_inc(ready.h, 1)
                body(eng, step)

            @block.tensor
            def _(eng):
                def step(g, h, first):
                    after(eng, hot, g + 1)
                    if not first:
                        after(eng, ready, g - 1)
                    for c in range(GRP):
                        eng.matmul(base[h][:, c * BLK:(c + 1) * BLK], soT[:, h, c * P:(c + 1) * P],
                                   s.before[:, ds(g * GRP + c, 1), :].rearrange("p a b -> p (a b)"),
                                   start=True, stop=True)
                        for t in range(RB):
                            mm = eng.matmul(relg[h][:, c * 12:(c + 1) * 12], tyT[:, h, t, c * P:(c + 1) * P],
                                            s.rel_parts[:, t].rearrange("p i r -> p (i r)"),
                                            start=(t == 0), stop=(t == RB - 1))
                    mm.then_inc(lookd.h, 1)
                body(eng, step)

            @block.gpsimd
            def _(eng):
                eng.wait_ge(init.h, i0 + 64)
                def step(g, h, first):
                    after(eng, ready, g + 1)
                    for c in range(GRP):
                        eng.indirect_dma_start(
                            s.sorted_d[:], bass.IndirectOffsetOnAxis(place[:, h, c:c + 1].bitcast(U32), 0),
                            recs[:, h, c, :], None).then_inc(sent[h].h, 16)
                body(eng, step)
                for h in range(2):
                    eng.wait_ge(sent[h].h, 16 * GRP * S // 2)


def load_sorted(p, s):
    nc = p.nc
    ctx = ExitStack()
    with ctx:
        mixed = p.sb("mixed", [P, CHUNKS], FP32, ctx)
        rows = p.sb("rows", [P, 3, KT, P], FP16, ctx)
        blocks = p.sb("blocks", [P, 2, CHUNKS], FP32, ctx)
        ps = p.ps("rowp", [P, 2, 512], ctx)
        ld, v, pe, act = (p.sem(x) for x in ("loaded", "dve", "pe", "act"))
        l0, v0, p0, a0 = ld.at, v.at, pe.at, act.at
        with p.block() as block:
            @block.sync
            def _(eng):
                eng.dma_start(s.e[:].rearrange("p k r -> p (k r)"),
                              s.sorted_d[0:P * CHUNKS, :].rearrange("(p k) r -> p (k r)", p=P)
                              ).then_inc(ld.h, 16)
                for i in range(2):
                    eng.dma_start(blocks[:, i], s.blocks_d[i, 0:CHUNKS].partition_broadcast(P)).then_inc(ld.h, 16)
                eng.wait_ge(act.h, a0 + 3 * KT)
                full = KT - 1
                for i in range(3):
                    to = s.pos_rows[i]
                    eng.dma_start(to[0:full * P * P].rearrange("(j p e) -> p j e", p=P, e=P),
                                  rows[:, i, 0:full, :]).then_inc(ld.h, 16)
                    n = CHUNKS - full * P
                    eng.dma_start(to[full * P * P:CHUNKS * P].rearrange("(p e) -> p e", e=P),
                                  rows[0:n, i, full, :]).then_inc(ld.h, 16)
                ld.at += 48 + 96
                eng.wait_ge(ld.h, ld.at)

            @block.vector
            def _(eng):
                eng.wait_ge(ld.h, l0 + 48)
                chain(eng, v, [lambda: eng.scalar_tensor_tensor(
                    mixed[:], s.e[:, :, 2], float(P), s.e[:, :, 0], ALU.mult, ALU.add)])
                chain(eng, v, [lambda: eng.memset(s.ctl[:], 0)])
                src, dst = 0, 1
                for table, now, field, which, times, plus in (
                        (0, 0, 0, src, 2 * D, 0), (0, 0, 4, dst, 2 * D, D), (0, 1, 8, dst, D, 0), (0, 1, 12, dst, 1, 0),
                        (1, 0, 0, src, 3 * D, 0), (1, 1, 4, dst, D, 0),
                        (2, 0, 0, dst, 2 * D, 0), (2, 1, 4, src, 2 * D, 0),
                        (3, 0, 0, src, 6, 0), (3, 0, 4, dst, 6, 0), (3, 0, 8, src, P, 0), (3, 1, 12, src, 2, 0)):
                    q = 32 * table
                    to = s.ctl[q:q + 1, now * CTL:(now + QUARTERS) * CTL].rearrange(
                        "o (t f) -> o t f", f=CTL)[:, :, field:field + 4]
                    of = blocks[q:q + 1, which, :].rearrange("o (t c) -> o t c", c=4)
                    eng.tensor_scalar(to, of, float(times), float(plus), ALU.mult, ALU.add).then_inc(v.h, 1)
                    v.at += 1

            @block.tensor
            def _(eng):
                eng.wait_ge(v.h, v0 + 1)
                for i in range(3):
                    for j in range(KT):
                        n = i * KT + j
                        k = min(P, CHUNKS - j * P)
                        of = mixed[:, j * P:j * P + k] if i == 2 else s.e[:, j * P:j * P + k, i]
                        after(eng, act, a0 + n - 1 if n >= 2 else 0)
                        eng.transpose(ps[0:k, n % 2, 0:P], of, p.ident[:]).then_inc(pe.h, 1)
                        pe.at += 1

            @block.scalar
            def _(eng):
                for i in range(3):
                    for j in range(KT):
                        n = i * KT + j
                        k = min(P, CHUNKS - j * P)
                        eng.wait_ge(pe.h, p0 + n + 1)
                        eng.copy(rows[0:k, i, j, :], ps[0:k, n % 2, 0:P]).then_inc(act.h, 1)
                        act.at += 1


GB = 5


def linear(p, s, of, K, layers, setup=None):
    nc = p.nc
    ctx = ExitStack()
    with ctx:
        turned = p.sb("turned_x", [P, GB * P], FP32, ctx)
        held = p.sb("held_x", [P, GB, P], FP32, ctx)
        tp = p.ps("tp", [P, 1024], ctx)
        op = [p.ps("op", [P, 1024], ctx) for _ in range(min(3, len(layers)))]
        pe, v, act, mm_done, pool = p.sem("pe"), p.sem("dve"), p.sem("act"), p.sem("node_products"), p.sem("pool")
        p0, v0, a0, m0, q0 = pe.at, v.at, act.at, mm_done.at, pool.at
        G, NL = BLK // GB, len(layers)
        NO = len(op)
        with p.block() as block:
            @block.gpsimd
            def _(eng):
                def step(g):
                    if not isinstance(g, int):
                        after(eng, pe, g + p0)
                    eng.tensor_copy(held[:], of[:, ds(g * GB, GB), :]).then_inc(pool.h, 1)
                step(0)
                with eng.Fori(1, G) as g:
                    step(g)
                pool.at += G

            @block.tensor
            def _(eng):
                with eng.Fori(0, G) as g:
                    after(eng, pool, g + (q0 + 1))
                    for b in range(GB):
                        mm = eng.transpose(tp[:, b * P:(b + 1) * P], held[:, b, :], p.ident[:])
                    mm.then_inc(pe.h, 1)
                    after(eng, v, g + (v0 + 1))
                    for n, (w, bias, N, func, out) in enumerate(layers):
                        if n >= NO:
                            after(eng, act, g * NL + (a0 + n - NO + 1))
                        for b in range(GB):
                            mm = eng.matmul(op[n % NO][:, b * N:(b + 1) * N], turned[0:K, b * P:(b + 1) * P],
                                            w, start=True, stop=bias is None)
                            if bias is not None:
                                mm = eng.matmul(op[n % NO][:, b * N:(b + 1) * N], p.ones[0:1, :], bias,
                                                start=False, stop=True)
                        mm.then_inc(mm_done.h, 1)
                    after(eng, act, g * NL + (a0 + NL))
                pe.at += G
                mm_done.at += G * NL

            @block.vector
            def _(eng):
                with eng.Fori(0, G) as g:
                    after(eng, pe, g + (p0 + 1))
                    eng.tensor_copy(turned[:], tp[:, 0:GB * P]).then_inc(v.h, 1)
                v.at += G

            @block.scalar
            def _(eng):
                with eng.Fori(0, G) as g:
                    for n, (w, bias, N, func, out) in enumerate(layers):
                        after(eng, mm_done, g * NL + (m0 + n + 1))
                        eng.activation(out[:, ds(g * GB, GB), :],
                                       op[n % NO][:, 0:GB * N].rearrange("p (b f) -> p b f", f=N),
                                       func).then_inc(act.h, 1)
                act.at += G * NL


def fetch(p, pairs):
    ld = p.sem("loaded")
    with p.block() as block:
        @block.sync
        def _(eng):
            for to, of in pairs:
                eng.dma_start(to, of).then_inc(ld.h, 16)
                ld.at += 16
            eng.wait_ge(ld.h, ld.at)


def on_vector(p, ops):
    v = p.sem("dve")
    with p.block() as block:
        @block.vector
        def _(eng):
            chain(eng, v, [lambda op=op: op(eng) for op in ops])


def split_stage(p, x, parts):
    on_vector(p, [
        lambda e: e.tensor_copy(parts[0], x),
        lambda e: e.tensor_tensor(x, x, parts[0], ALU.subtract),
        lambda e: e.tensor_copy(parts[1], x),
        lambda e: e.tensor_tensor(parts[2], x, parts[1], ALU.subtract)])


def layernorm(p, x, out, tmp, gamma=None, beta=None):
    ctx = ExitStack()
    with ctx:
        mean = p.sb("mean", [P, BLK], FP32, ctx)
        var = p.sb("var", [P, BLK], FP32, ctx)
        v, act = p.sem("dve"), p.sem("act")
        v0, a0 = v.at, act.at
        B = lambda t: t[:].unsqueeze(2).to_broadcast([P, BLK, D])
        R = lambda t: t.unsqueeze(1).to_broadcast([P, BLK, D])
        with p.block() as block:
            @block.vector
            def _(eng):
                chain(eng, v, [
                    lambda: eng.tensor_reduce(mean[:], x, AX.X, ALU.add),
                    lambda: eng.tensor_scalar(mean[:], mean[:], 1.0 / D, None, ALU.mult),
                    lambda: eng.tensor_tensor(out, x, B(mean), ALU.subtract),
                    lambda: eng.tensor_tensor(tmp, out, out, ALU.mult),
                    lambda: eng.tensor_reduce(var[:], tmp, AX.X, ALU.add),
                    lambda: eng.tensor_scalar(var[:], var[:], 1.0 / D, 1e-5, ALU.mult, ALU.add)])
                eng.wait_ge(act.h, a0 + 1)
                chain(eng, v, [
                    lambda: eng.reciprocal(var[:], var[:]),
                    lambda: eng.tensor_tensor(out, out, B(var), ALU.mult)])
                if gamma is not None:
                    chain(eng, v, [
                        lambda: eng.tensor_tensor(out, out, R(gamma), ALU.mult),
                        lambda: eng.tensor_tensor(out, out, R(beta), ALU.add)])

            @block.scalar
            def _(eng):
                eng.wait_ge(v.h, v0 + 6)
                eng.sqrt(var[:], var[:]).then_inc(act.h, 1)
                act.at += 1


def quarters(eng, step):
    for t in range(4):
        step(t, t)
    with eng.Fori(1, (QUARTERS - 1) // 4) as i:
        for c in range(4):
            step(i * 4 + c, c)
    step(QUARTERS - 1, (QUARTERS - 1) % 4)


def edge_pass(p, s, rows, field, hot_dt, table, spans, banks, hot_parts, gather, scatter, G_shape,
              vector=None, scalar=None, finish=None, pool=None, free_when_made=False, H=2):
    nc = p.nc
    ctx = ExitStack()
    NR, NH = len(rows), len(hot_parts)
    with ctx:
        idx = p.sb("idx", [P, 4, NR, 4 * P], FP16, ctx)
        hotT = p.sb("hotT", [P, 2, NH, 4 * P], BF16, ctx)
        hot = p.sb("hot", [P, 2, 4, P], hot_dt, ctx)
        place = p.sb("place", [P, 2, 4], FP32, ctx)
        placed = p.sem("placed")
        pl0 = placed.at
        if banks:
            acc = p.ps("acc", [P, banks * 512], ctx)
        G = G_shape(ctx)
        idx_in = [p.sem(f"positions_{c}") for c in range(4)]
        turned, hots = p.sem("gather_hot"), p.sem("scatter_hot")
        gathered, taken, made, scattered = (p.sem(x) for x in ("gathered", "taken", "made", "scattered"))
        i0 = [x.at for x in idx_in]
        tu0, h0, g0, t0, m0, sc0 = (x.at for x in (turned, hots, gathered, taken, made, scattered))
        pairs = H * QUARTERS
        Q = QUARTERS

        def later(eng, sem, base, value):
            if isinstance(value, int):
                if value > 0:
                    after(eng, sem, base + value)
            else:
                after(eng, sem, value + base)

        def scatter_positions(eng, t, c, field):
            eng.tensor_copy(place[:, c % 2].unsqueeze(2), s.e[:, ds(t * 4, 4), field:field + 1]).then_inc(placed.h, 1)
            later(eng, placed, pl0, t + 1)

        env = dict(scatter_positions=scatter_positions, place=place, idx=idx, hotT=hotT, hot=hot, acc=acc if banks else None, G=G, later=later,
                   gathered=gathered, taken=taken, made=made, scattered=scattered, hots=hots,
                   g0=g0, t0=t0, m0=m0, sc0=sc0, h0=h0)
        with p.block() as block:
            @block.sync
            def _(eng):
                def step(t, c):
                    if not isinstance(t, int) or t >= 4:
                        later(eng, turned, tu0, t - 3)
                    for r in range(NR):
                        eng.dma_start(idx[:, c, r], rows[r][ds(t * (4 * P), 4 * P)].partition_broadcast(P)
                                      ).then_inc(idx_in[c].h, 16)
                quarters(eng, step)
                for c in range(4):
                    n = (Q - c + 3) // 4
                    idx_in[c].at += 16 * NR * n

            @block.gpsimd
            def _(eng):
                def step(t, c):
                    later(eng, hots, h0, t - 1)
                    eng.tensor_copy(place[:, c % 2].unsqueeze(2), s.e[:, ds(t * 4, 4), field:field + 1]
                                    ).then_inc(placed.h, 1)
                if pool:
                    quarters(eng, lambda t, c: pool(eng, t, c, env))
                elif field is not None:
                    quarters(eng, step)
                    hots.at += Q

            @block.vector
            def _(eng):
                def one_hots(t, c, first=False):
                    if isinstance(t, int):
                        later(eng, idx_in[c], i0[c], 16 * NR * (t // 4 + 1))
                    else:
                        later(eng, idx_in[c], i0[c], (t - c) * (4 * NR) + 16 * NR)
                    later(eng, gathered, g0, t * H - H)
                    for n, (r, first) in enumerate(hot_parts):
                        op = eng.tensor_scalar(hotT[:, c % 2, n], idx[:, c, r], p.col[:, first:first + 1], None,
                                               ALU.is_equal)
                    op.then_inc(turned.h, 1)
                def scatter_hots(t, c):
                    later(eng, scattered, sc0, t * H - H)
                    later(eng, placed, pl0, t + 1)
                    for q in range(4):
                        op = eng.tensor_scalar(hot[:, c % 2, q], p.row16[:], place[:, c % 2, q:q + 1], None,
                                               ALU.is_equal)
                    op.then_inc(hots.h, 1)
                def step(t, c):
                    if not (isinstance(t, int) and t == Q - 1):
                        one_hots(t + 1, (c + 1) % 4)
                    if field is not None:
                        scatter_hots(t, c)
                    if vector:
                        vector(eng, t, c, env)
                one_hots(0, 0)
                quarters(eng, step)
                turned.at += Q
                if finish and "vector" in finish:
                    eng.wait_ge(scattered.h, sc0 + pairs)
                    finish["vector"](eng, env)

            @block.scalar
            def _(eng):
                if scalar:
                    quarters(eng, lambda t, c: scalar(eng, t, c, env))
                if finish and "scalar" in finish:
                    eng.wait_ge(scattered.h, sc0 + pairs)
                    finish["scalar"](eng, env)

            @block.tensor
            def _(eng):
                for b in range(banks):
                    eng.matmul(acc[:, b * 512:(b + 1) * 512], s.zeros[:, 0:P], s.zeros[:], start=True, stop=True,
                               skip_group_check=True)
                def step(t, c, gathers=True, scatters=True):
                    regs, at = [], []
                    for first, most in spans:
                        r = s.regs[len(regs):len(regs) + 4 * len(most)]
                        eng.load(r, s.ctl[32 * table:32 * table + 1, ds(t * CTL + first, len(r))])
                        regs += r
                        at += [eng.snap(x, min_val=0, max_val=most[n // 4]) for n, x in enumerate(r)]
                    if gathers:
                        later(eng, turned, tu0, t + 1)
                    if scatters and field is not None:
                        later(eng, hots, h0, t)
                    for h in range(H):
                        if gathers:
                            later(eng, made if free_when_made else taken, m0 if free_when_made else t0,
                                  t * H + h - H + 1)
                            gather(eng, c, h, at, env).then_inc(gathered.h, 1)
                        if scatters:
                            later(eng, made, m0, t * H + h - H + 1)
                            scatter(eng, c, h, at, env).then_inc(scattered.h, 1)
                step(0, 0, scatters=False)
                for t in range(1, 4):
                    step(t, t, scatters=scatter is not None)
                with eng.Fori(1, (Q - 1) // 4) as i:
                    for c in range(4):
                        step(i * 4 + c, c, scatters=scatter is not None)
                step(Q - 1, 0, scatters=scatter is not None)
                if scatter is not None:
                    step(Q, 1, gathers=False)
                    scattered.at += pairs
                gathered.at += pairs
        placed.at += Q
        if not free_when_made:
            taken.at += pairs
        if scatter is not None:
            made.at += pairs


def gnn_layer(p, s, l, degrees):
    ctx = ExitStack()
    with ctx:
        terms = p.sb("terms", [P, 2, 4, D], FP32, ctx)
        sums = p.sb("sums", [P, 4, 2, D], FP32, ctx)
        msgs = p.sb("msgs", [P, 4, 2, D], FP32, ctx)
        termed, relu_done = p.sem("termed"), p.sem("added")
        te0, ad0 = termed.at, relu_done.at

        def gather(eng, c, h, at, env):
            for k in range(2):
                q = 2 * h + k
                n = 0
                for side in range(2):
                    for part in range(3):
                        mm = eng.matmul(env["G"][h][:, k * D:(k + 1) * D], env["hotT"][:, c % 2, side, q * P:(q + 1) * P],
                                        s.tables[part][:, ds(at[4 * side + q], D)], start=(n == 0), stop=(n == 5))
                        n += 1
            return mm

        def scatter(eng, c, h, at, env):
            j = (2 * (c - 1) + h) % 4
            for k in range(2):
                q = 2 * h + k
                mm = eng.matmul(env["acc"][:, ds(at[8 + q], D)], env["hot"][:, (c - 1) % 2, q, :], msgs[:, j, k, :],
                                start=False, stop=False, skip_group_check=True)
                if degrees:
                    mm = eng.matmul(env["acc"][:, 4 * 512:5 * 512][:, ds(at[12 + q], 1)], env["hot"][:, (c - 1) % 2, q, :],
                                    p.ones[:, 0:1], start=False, stop=False, skip_group_check=True)
            return mm

        def vector(eng, t, c, env):
            eng.tensor_tensor(terms[:, c % 2], s.e[:, ds(t * 4, 4), 3:4].to_broadcast([P, 4, D]),
                              s.we[:, l].unsqueeze(1).to_broadcast([P, 4, D]), ALU.mult).then_inc(termed.h, 1)
            for h in range(2):
                j = (2 * c + h) % 4
                if h == 0:
                    env["later"](eng, termed, te0, t + 1)
                env["later"](eng, env["gathered"], env["g0"], t * 2 + h + 1)
                env["later"](eng, env["made"], env["m0"], t * 2 + h - 3)
                eng.tensor_tensor(sums[:, j], env["G"][h][:, 0:2 * D].rearrange("p (k f) -> p k f", f=D),
                                  terms[:, c % 2, 2 * h:2 * h + 2], ALU.add).then_inc(env["taken"].h, 1)

        def scalar(eng, t, c, env):
            for h in range(2):
                j = (2 * c + h) % 4
                env["later"](eng, env["taken"], env["t0"], t * 2 + h + 1)
                env["later"](eng, env["scattered"], env["sc0"], t * 2 + h - 3)
                eng.activation(msgs[:, j], sums[:, j], ACT.Relu).then_inc(env["made"].h, 1)

        def finish(eng, env):
            act = p.sem("act")
            eng.copy(s.cat[:, :, D:2 * D], env["acc"][:, 0:BLK * D].rearrange("p (b f) -> p b f", f=D)).then_inc(act.h, 1)
            act.at += 1
            if degrees:
                eng.copy(s.deg[:], env["acc"][:, 2048:2048 + BLK]).then_inc(act.h, 1)
                act.at += 1

        edge_pass(p, s, [s.pos_rows[0], s.pos_rows[1]], 1, FP32, 0,
                  [(0, [LAST * P, LAST * P + D]), (8, [LAST * D, LAST] if degrees else [LAST * D])], 5 if degrees else 4, [(0, 0), (1, 0)], gather, scatter,
                  lambda c: [p.ps("G", [P, 512], c) for _ in range(2)], vector, scalar, {"scalar": finish})
        termed.at += QUARTERS


def sum_pass(p, s, relations=False):
    ctx = ExitStack()
    with ctx:
        msgs = p.sb("msgs", [P, 4, 2, 3 * D], BF16, ctx)

        def gather(eng, c, h, at, env):
            n = RELS if relations else 1
            for k in range(2):
                q = 2 * h + k
                for r in range(n):
                    mm = eng.matmul(env["G"][h][:, k * 3 * D:(k + 1) * 3 * D],
                                    env["hotT"][:, c % 2, r, q * P:(q + 1) * P],
                                    s.wide[r][:, ds(at[q], 3 * D)], start=(r == 0), stop=(r == n - 1))
            return mm

        def scatter(eng, c, h, at, env):
            j = (2 * (c - 1) + h) % 4
            for k in range(2):
                q = 2 * h + k
                for part in range(3):
                    mm = eng.matmul(env["acc"][:, ds(at[4 + q], D)], env["hot"][:, (c - 1) % 2, q, :],
                                    msgs[:, j, k, part * D:(part + 1) * D], start=False, stop=False,
                                    skip_group_check=True)
            return mm

        def scalar(eng, t, c, env):
            for h in range(2):
                j = (2 * c + h) % 4
                env["later"](eng, env["gathered"], env["g0"], t * 2 + h + 1)
                env["later"](eng, env["scattered"], env["sc0"], t * 2 + h - 3)
                op = eng.copy(msgs[:, j], env["G"][h][:, 0:6 * D].rearrange("p (k f) -> p k f", f=3 * D))
                op.then_inc(env["made"].h, 1)

        def finish(eng, env):
            act = p.sem("act")
            eng.copy(s.cat[:, :, D:2 * D], env["acc"][:, 0:BLK * D].rearrange("p (b f) -> p b f", f=D)).then_inc(act.h, 1)
            act.at += 1

        edge_pass(p, s, [s.pos_rows[2 if relations else 0]], 1, BF16, 1, [(0, [LAST * 3 * D, LAST * D])], 4,
                  [(0, r) for r in range(RELS if relations else 1)], gather, scatter,
                  lambda c: [p.ps("G", [P, 512], c) for _ in range(2)], None, scalar, {"scalar": finish},
                  free_when_made=True)


def score_pass(p, s, l):
    ctx = ExitStack()
    with ctx:
        sums = p.sb("sums", [P, 2, 4, HEADS], FP32, ctx)
        offs = p.sb("offs", [P, 2, 4, P], FP32, ctx)
        same = p.sb("same", [P, 2, 4, P], FP32, ctx)
        steps, topped, offset, sames = (p.sem(x) for x in ("score_steps", "topped", "offset", "same"))
        sd0, to0, of0, sa0 = steps.at, topped.at, offset.at, sames.at

        def gather(eng, c, h, at, env):
            for k in range(2):
                q = 2 * h + k
                for side in range(2):
                    mm = eng.matmul(env["G"][h][:, k * 6:(k + 1) * 6], env["hotT"][:, c % 2, side, q * P:(q + 1) * P],
                                    s.small[side][:, ds(at[4 * side + q], 6)], start=(side == 0), stop=(side == 1))
            return mm

        def pool(eng, t, c, env):
            env["later"](eng, topped, to0, (t * 8) - 8)
            env["scatter_positions"](eng, t, c, 0)
            for q in range(4):
                op = eng.tensor_scalar(same[:, c % 2, q], p.row[:], env["place"][:, c % 2, q:q + 1], None, ALU.is_equal)
            op.then_inc(sames.h, 1)
            env["later"](eng, sames, sa0, t + 1)
            eng.tensor_scalar(offs[:, c % 2], same[:, c % 2], BIG, -BIG, ALU.mult, ALU.add).then_inc(offset.h, 1)

        def vector(eng, t, c, env):
            o = c % 2
            for h in range(2):
                env["later"](eng, env["gathered"], env["g0"], t * 2 + h + 1)
                eng.tensor_reduce(sums[:, o, 2 * h:2 * h + 2], env["G"][h][:, 0:12].rearrange(
                    "p (k i r) -> p k r i", i=3, r=HEADS), AX.X, ALU.add).then_inc(env["taken"].h, 1)
            env["later"](eng, env["taken"], env["t0"], t * 2 + 2)
            eng.tensor_tensor(sums[:, o], sums[:, o], s.e[:, ds(t * 4, 4), 4 + 2 * l:6 + 2 * l],
                              ALU.add).then_inc(steps.h, 1)
            env["later"](eng, steps, sd0, t * 2 + 1)
            eng.scalar_tensor_tensor(sums[:, o], sums[:, o], 0.01, sums[:, o], ALU.mult, ALU.max).then_inc(steps.h, 1)
            env["later"](eng, steps, sd0, t * 2 + 2)
            eng.tensor_copy(s.score[:, ds(t * 4, 4), :], sums[:, o])
            eng.load(s.vregs, s.ctl[96:97, ds(t * CTL + 8, 4)])
            env["later"](eng, offset, of0, t + 1)
            for q in range(4):
                at = eng.snap(s.vregs[q], min_val=0, max_val=LAST * P)
                for h in range(HEADS):
                    if not (isinstance(t, int) and t == 0 and q == 0):
                        env["later"](eng, topped, to0, t * 8 + (2 * q + h - 1))
                    best = s.top[h][:, ds(at, P)]
                    eng.scalar_tensor_tensor(best, offs[:, o, q], sums[:, o, q, h:h + 1], best,
                                             ALU.add, ALU.max).then_inc(topped.h, 1)

        edge_pass(p, s, [s.pos_rows[0], s.pos_rows[1]], None, BF16, 3, [(0, [LAST * 6, LAST * 6])], 0,
                  [(0, 0), (1, 0)], gather, None, lambda c: [p.ps("G", [P, 512], c) for _ in range(2)],
                  vector, pool=pool)
        steps.at += 2 * QUARTERS
        topped.at += 8 * QUARTERS
        offset.at += QUARTERS
        sames.at += QUARTERS


def reduce_tops(p, s):
    ctx = ExitStack()
    with ctx:
        ps = p.ps("tops", [P, 2, HEADS * P], ctx)
        held = p.sb("held_t", [P, HEADS, P], FP32, ctx)
        pe, v, pool = p.sem("pe"), p.sem("dve"), p.sem("pool")
        p0, v0, q0 = pe.at, v.at, pool.at
        with p.block() as block:
            @block.gpsimd
            def _(eng):
                def step(b):
                    if not isinstance(b, int):
                        after(eng, pe, b + p0)
                    for h in range(HEADS):
                        eng.tensor_copy(held[:, h, :], s.top[h][:, ds(b * P, P)]).then_inc(pool.h, 1)
                step(0)
                with eng.Fori(1, BLK) as b:
                    step(b)
                pool.at += HEADS * BLK

            @block.tensor
            def _(eng):
                with eng.Fori(0, BLK) as b:
                    after(eng, pool, b * HEADS + (q0 + HEADS))
                    for h in range(HEADS):
                        mm = eng.transpose(ps[:, 0, h * P:(h + 1) * P], held[:, h, :], p.ident[:])
                    mm.then_inc(pe.h, 1)
                    after(eng, v, b + (v0 + 1))
                pe.at += BLK

            @block.vector
            def _(eng):
                with eng.Fori(0, BLK) as b:
                    after(eng, pe, b + (p0 + 1))
                    eng.tensor_reduce(s.most[:, ds(b, 1), :].rearrange("p o h -> p (o h)"),
                                      ps[:, 0, :].rearrange("p (h e) -> p h e", e=P), AX.X, ALU.max
                                      ).then_inc(v.h, 1)
                v.at += BLK


def exp_pass(p, s):
    ctx = ExitStack()
    with ctx:
        sums = p.sb("sums", [P, 4, 2, HEADS], FP32, ctx)
        less = p.sb("less", [P, 4, 2, HEADS], FP32, ctx)
        msgs = p.sb("msgs", [P, 4, 2, HEADS], FP32, ctx)
        lessed = p.sem("lessed")
        le0 = lessed.at

        def gather(eng, c, h, at, env):
            for k in range(2):
                q = 2 * h + k
                mm = eng.matmul(env["G"][h][:, k * 6:(k + 1) * 6], env["hotT"][:, c % 2, 0, q * P:(q + 1) * P],
                                s.small[0][:, ds(at[q], 6)], start=True, stop=True)
            return mm

        def scatter(eng, c, h, at, env):
            j = (2 * (c - 1) + h) % 4
            for k in range(2):
                q = 2 * h + k
                mm = eng.matmul(env["acc"][:, ds(at[4 + q], HEADS)], env["hot"][:, (c - 1) % 2, q, :], msgs[:, j, k, :],
                                start=False, stop=False, skip_group_check=True)
            return mm

        def vector(eng, t, c, env):
            for h in range(2):
                j = (2 * c + h) % 4
                env["later"](eng, env["gathered"], env["g0"], t * 2 + h + 1)
                eng.tensor_reduce(sums[:, j], env["G"][h][:, 0:12].rearrange(
                    "p (k i r) -> p k r i", i=3, r=HEADS), AX.X, ALU.add).then_inc(env["taken"].h, 1)
                env["later"](eng, env["taken"], env["t0"], t * 2 + h + 1)
                env["later"](eng, env["made"], env["m0"], t * 2 + h - 3)
                eng.tensor_tensor(less[:, j], s.score[:, ds(t * 4 + 2 * h, 2), :], sums[:, j],
                                  ALU.subtract).then_inc(lessed.h, 1)

        def scalar(eng, t, c, env):
            for h in range(2):
                j = (2 * c + h) % 4
                env["later"](eng, lessed, le0, t * 2 + h + 1)
                env["later"](eng, env["scattered"], env["sc0"], t * 2 + h - 3)
                eng.activation(s.score[:, ds(t * 4 + 2 * h, 2), :], less[:, j], ACT.Exp)
                eng.activation(msgs[:, j], less[:, j], ACT.Exp).then_inc(env["made"].h, 1)

        def finish(eng, env):
            act = p.sem("act")
            eng.copy(s.z[:].rearrange("p b h -> p (b h)"), env["acc"][:, 0:BLK * HEADS]).then_inc(act.h, 1)
            act.at += 1

        edge_pass(p, s, [s.pos_rows[0]], 0, FP32, 3, [(0, [LAST * 6]), (12, [LAST * 2])], 1, [(0, 0)],
                  gather, scatter, lambda c: [p.ps("G", [P, 512], c) for _ in range(2)], vector, scalar,
                  {"scalar": finish})
        lessed.at += 2 * QUARTERS


def spread_pass(p, s, out):
    ctx = ExitStack()
    W = HEADS * D
    with ctx:
        msgs = p.sb("msgs", [P, 2, 4, W], FP32, ctx)

        def gather(eng, c, h, at, env):
            for q in range(4):
                for part in range(3):
                    mm = eng.matmul(env["G"][:, q * W:(q + 1) * W], env["hotT"][:, c % 2, 0, q * P:(q + 1) * P],
                                    s.tables[part][:, ds(at[q], W)], start=(part == 0), stop=(part == 2))
            return mm

        def scatter(eng, c, h, at, env):
            for q in range(4):
                mm = eng.matmul(env["acc"][:, ds(at[4 + q], W)], env["hot"][:, (c - 1) % 2, q, :], msgs[:, (c - 1) % 2, q, :],
                                start=False, stop=False, skip_group_check=True)
            return mm

        def vector(eng, t, c, env):
            env["later"](eng, env["gathered"], env["g0"], t + 1)
            env["later"](eng, env["scattered"], env["sc0"], t - 1)
            eng.tensor_tensor(msgs[:, c % 2].rearrange("p q (r f) -> p (q r) f", f=D),
                              env["G"].rearrange("p (k f) -> p k f", f=D),
                              s.score[:, ds(t * 4, 4), :].rearrange("p k r -> p (k r)").unsqueeze(2)
                              .to_broadcast([P, 4 * HEADS, D]), ALU.mult).then_inc(env["made"].h, 1)

        def finish(eng, env):
            v = p.sem("dve")
            four = lambda x: x.rearrange("p (b r f) -> p b r f", r=HEADS, f=D)
            o = out.rearrange("p b (r f) -> p b r f", f=D)
            chain(eng, v, [
                lambda: eng.tensor_tensor(o, four(env["acc"][:, 0:BLK * W]),
                                          s.rz[:].unsqueeze(3).to_broadcast([P, BLK, HEADS, D]), ALU.mult),
                lambda: eng.tensor_tensor(o, o, s.ah[:].unsqueeze(2).to_broadcast([P, BLK, HEADS, D]), ALU.add)])

        edge_pass(p, s, [s.pos_rows[1]], 0, FP32, 2, [(0, [LAST * W, LAST * W])], 7, [(0, 0)],
                  gather, scatter, lambda c: p.ps("G", [P, 512], c)[:, :], vector, None, {"vector": finish},
                  free_when_made=True, H=1)


def message_net(p, s):
    ins = p.ins
    ctx = ExitStack()
    with ctx:
        s.tables = [p.sb(f"table_m{i}", [P, BLK * P], BF16, ctx) for i in range(3)]
        u = p.sb("u_m", [P, BLK, P], FP32, ctx)
        wsd = p.sb("wsd", [D, 3, 2, D], FP32, ctx)
        wn = p.sb("wn", [P, 3, D], FP32, ctx)
        bsd = p.sb("bsd", [1, 3, 2, D], FP32, ctx)
        bn = p.sb("bn", [1, 3, D], FP32, ctx)
        s.we = p.sb("we", [P, 3, D], FP32, ctx)
        ew = ins["L0_gnn_edge_W"]
        on_vector(p, [lambda e: e.memset(bsd[:], 0.0), lambda e: e.tensor_copy(s.cat[:, :, 0:D], s.x[:])])
        fetch(p, [(wsd[:, l], ew[l, 0:2 * D, :].rearrange("(s d) f -> d s f", d=D)) for l in range(3)]
              + [(wn[:], ins["L0_gnn_node_W"].rearrange("l k f -> k l f")),
                 (bsd[:, :, 0, :], ins["L0_gnn_edge_b"].unsqueeze(0)),
                 (bn[:], ins["L0_gnn_node_b"].unsqueeze(0))]
              + [(s.we[:, l], ew[l, 2 * D, :].partition_broadcast(P)) for l in range(3)])
        for l in range(3):
            linear(p, s, s.cat, D, [(wsd[:, l].rearrange("d s f -> d (s f)"),
                                     bsd[:, l].rearrange("o s f -> o (s f)"), 2 * D, ACT.Copy, u)])
            split_stage(p, u[:].rearrange("p b f -> p (b f)"), [t[:] for t in s.tables])
            gnn_layer(p, s, l, l == 0)
            linear(p, s, s.cat, P, [(wn[:, l], bn[:, l], D, ACT.Relu, s.cat[:, :, 0:D])])
        on_vector(p, [lambda e: e.tensor_tensor(s.cat[:, :, 0:D], s.cat[:, :, 0:D], s.x[:], ALU.add)])
        layernorm(p, s.cat[:, :, 0:D], s.x[:], s.cat[:, :, D:2 * D])


def relation_net(p, s):
    ins = p.ins
    ctx = ExitStack()
    with ctx:
        s.wide = [p.sb(f"wide{r}", [P, BLK * 3 * D], BF16, ctx) for r in range(RELS)]
        own = p.sb("own", [P, BLK, D], FP32, ctx)
        first = ExitStack()
        with first:
            u = p.sb("u_r", [P, BLK, P], FP32, first)
            wenc = p.sb("wenc", [D, D], FP32, first)
            wself = p.sb("wself", [D, D], FP32, first)
            wrel = p.sb("wrel", [D, RELS // 2, 2, D], FP32, first)
            bs = p.sb("bs_r", [1, 2, D], FP32, first)
            on_vector(p, [lambda e: e.tensor_copy(s.cat[:, :, 0:D], s.x[:])])
            fetch(p, [(wenc[:], ins["L1_gnn_W_enc"]), (wself[:], ins["L1_gnn_W_self"]),
                      (wrel[:].rearrange("d a b f -> d (a b) f"), ins["L1_gnn_W_rel"].rearrange("r d f -> d r f")),
                      (bs[:, 0], ins["L1_gnn_b_enc"].unsqueeze(0)), (bs[:, 1], ins["L1_gnn_bias"].unsqueeze(0))])
            linear(p, s, s.cat, D, [(wenc[:], bs[:, 0], D, ACT.Relu, s.cat[:, :, 0:D])])
            linear(p, s, s.cat, D, [(wself[:], bs[:, 1], D, ACT.Copy, own)])
            for i in range(RELS // 2):
                linear(p, s, s.cat, D, [(wrel[:, i].rearrange("d b f -> d (b f)"), None, 2 * D, ACT.Copy, u)])
                for k in range(2):
                    w = s.wide[2 * i + k][:].rearrange("p (b q f) -> p b q f", q=3, f=D)
                    split_stage(p, u[:, :, k * D:(k + 1) * D], [w[:, :, q, :] for q in range(3)])
        sum_pass(p, s, relations=True)
        a, b = s.cat[:, :, 0:D], s.cat[:, :, D:2 * D]
        on_vector(p, [lambda e: e.tensor_tensor(b, b, own[:], ALU.add),
                      lambda e: e.tensor_scalar(b, b, 0.0, None, ALU.max),
                      lambda e: e.tensor_tensor(a, a, b, ALU.add),
                      lambda e: e.tensor_tensor(a, a, s.x[:], ALU.add)])
        layernorm(p, a, s.x[:], b)


def sage_net(p, s):
    ins = p.ins
    ctx = ExitStack()
    with ctx:
        s.wide = [p.sb("wide_s", [P, BLK * 3 * D], BF16, ctx)]
        u = p.sb("u_s", [P, BLK, D], FP32, ctx)
        w = p.sb("w_s", [P, 2, D], FP32, ctx)
        bs = p.sb("bs_s", [1, 2, D], FP32, ctx)
        a, b = s.cat[:, :, 0:D], s.cat[:, :, D:2 * D]
        on_vector(p, [lambda e: e.tensor_copy(a, s.x[:]),
                      lambda e: e.tensor_scalar(s.deg[:], s.deg[:], 1.0, None, ALU.max),
                      lambda e: e.reciprocal(s.deg[:], s.deg[:])])
        fetch(p, [(w[0:D, 0], ins["L2_gnn_W1r"]), (w[D:P, 0], ins["L2_gnn_W1l"]),
                  (w[0:D, 1], ins["L2_gnn_W2r"]), (w[D:P, 1], ins["L2_gnn_W2l"]),
                  (bs[:, 0], ins["L2_gnn_b1"].unsqueeze(0)), (bs[:, 1], ins["L2_gnn_b2"].unsqueeze(0))])
        wide = s.wide[0][:].rearrange("p (b q f) -> p b q f", q=3, f=D)
        for i in range(2):
            on_vector(p, [lambda e: e.tensor_copy(u[:], a)])
            split_stage(p, u[:], [wide[:, :, q, :] for q in range(3)])
            sum_pass(p, s)
            on_vector(p, [lambda e: e.tensor_tensor(b, b, s.deg[:].unsqueeze(2).to_broadcast([P, BLK, D]), ALU.mult)])
            linear(p, s, s.cat, P, [(w[:, i], bs[:, i], D, ACT.Relu, a)])
        on_vector(p, [lambda e: e.tensor_tensor(a, a, s.x[:], ALU.add)])
        layernorm(p, a, s.x[:], b)


def attention_net(p, s):
    ins = p.ins
    ctx = ExitStack()
    W = HEADS * D
    with ctx:
        s.score = p.sb("score", [P, CHUNKS, HEADS], FP32, ctx)
        ent = p.sb("ent", [P, BLK, D], FP32, ctx)
        s.ah = p.sb("ah", [P, BLK, D], FP32, ctx)
        s.most = p.sb("most", [P, BLK, HEADS], FP32, ctx)
        s.z = p.sb("z", [P, BLK, HEADS], FP32, ctx)
        s.rz = p.sb("rz", [P, BLK, HEADS], FP32, ctx)
        nodes = [p.sb(f"nodes{i}", [P, BLK, HEADS], FP32, ctx) for i in range(2)]
        s.small = [p.sb(f"small{i}", [P, BLK * 6], BF16, ctx) for i in range(2)]
        wht = p.sb("wht", [D, LAYERS, 2, W], FP32, ctx)
        wo = p.sb("wo", [P, LAYERS, D], FP32, ctx)
        att = p.sb("att_ht", [P, LAYERS, 2, W], FP32, ctx)
        gb = p.sb("gb", [P, LAYERS, 2, D], FP32, ctx)
        fetch(p, [(wht[:, :, 0], ins["L3_gnn_W_h"].rearrange("l d w -> d l w")),
                  (wht[:, :, 1], ins["L3_gnn_W_t"].rearrange("l d w -> d l w")),
                  (wo[:], ins["L3_gnn_W_o"].rearrange("l k f -> k l f"))]
              + [x for l in range(LAYERS) for x in (
                  (att[:, l, 0], ins["L3_gnn_att_h"][l].rearrange("h d -> (h d)").partition_broadcast(P)),
                  (att[:, l, 1], ins["L3_gnn_att_t"][l].rearrange("h d -> (h d)").partition_broadcast(P)),
                  (gb[:, l, 0], ins["L3_gnn_ln_gamma"][l].partition_broadcast(P)),
                  (gb[:, l, 1], ins["L3_gnn_ln_beta"][l].partition_broadcast(P)))])
        small = [t[:].rearrange("p (b i r) -> p b i r", i=3, r=HEADS) for t in s.small]
        on_vector(p, [lambda e: e.tensor_copy(ent[:], s.x[:])])
        for l in range(LAYERS):
            h = s.cat[:, :, 0:D]
            layernorm(p, ent[:], h, s.cat[:, :, D:2 * D], gb[:, l, 0], gb[:, l, 1])
            on_vector(p, [lambda e: e.tensor_scalar(s.ah[:], h, 0.15, None, ALU.mult)])
            first = ExitStack()
            with first:
                s.top = [p.sb(f"top{l}{i}", [P, BLK * P], FP32, first) for i in range(HEADS)]
                u = [p.sb(f"u_a{l}{i}", [P, BLK, P], FP32, first) for i in range(2)]
                linear(p, s, s.cat, D, [(wht[:, l, i], None, W, ACT.Tanh, u[i]) for i in range(2)])
                for i in range(2):
                    on_vector(p, [
                        lambda e: e.tensor_tensor(u[i][:], u[i][:], att[:, l, i].unsqueeze(1).to_broadcast(
                            [P, BLK, W]), ALU.mult),
                        lambda e: e.tensor_reduce(nodes[i][:].rearrange("p b r -> p (b r)"),
                                                  u[i][:].rearrange("p b (r f) -> p (b r) f", f=D), AX.X, ALU.add),
                        lambda e: e.memset(s.top[i][:], -BIG)])
                    split_stage(p, nodes[i][:], [small[i][:, :, q, :] for q in range(3)])
                score_pass(p, s, l)
                reduce_tops(p, s)
            split_stage(p, s.most[:], [small[0][:, :, q, :] for q in range(3)])
            exp_pass(p, s)
            on_vector(p, [lambda e: e.tensor_scalar(s.z[:], s.z[:], 0.5, None, ALU.max),
                          lambda e: e.reciprocal(s.z[:], s.z[:]),
                          lambda e: e.tensor_scalar(s.rz[:], s.z[:], 0.85, None, ALU.mult)])
            second = ExitStack()
            with second:
                s.tables = [p.sb(f"table_a{l}{i}", [P, BLK * P], BF16, second) for i in range(3)]
                u = p.sb(f"u_b{l}", [P, BLK, P], FP32, second)
                four = lambda x: x.rearrange("p b (r f) -> p b r f", f=D)
                on_vector(p, [lambda e: e.tensor_copy(four(u[:]), h.unsqueeze(2).to_broadcast([P, BLK, HEADS, D]))])
                for k in range(3):
                    split_stage(p, u[:].rearrange("p b f -> p (b f)"), [t[:] for t in s.tables])
                    spread_pass(p, s, u[:])
                linear(p, s, u, P, [(wo[:, l], None, D, ACT.Copy, s.cat[:, :, 0:D])])
                on_vector(p, [lambda e: e.tensor_tensor(ent[:], ent[:], s.cat[:, :, 0:D], ALU.add)])
        on_vector(p, [lambda e: e.tensor_tensor(ent[:], ent[:], s.x[:], ALU.add)])
        layernorm(p, ent[:], s.x[:], s.cat[:, :, 0:D])


def load_nodes(p, s):
    v, ld = p.sem("dve"), p.sem("loaded")
    v0 = v.at
    full, rest = BLK - 1, NODES - (BLK - 1) * P
    with p.block() as block:
        @block.vector
        def _(eng):
            chain(eng, v, [lambda: eng.memset(s.x[:], 0.0), lambda: eng.memset(s.cat[:], 0.0),
                           lambda: eng.memset(s.zeros[:], 0.0)])

        @block.sync
        def _(eng):
            eng.wait_ge(v.h, v0 + 3)
            x = p.ins["x"]
            eng.dma_start(s.x[:, 0:full, :], x[0:full * P, :].rearrange("(b q) f -> q b f", q=P)).then_inc(ld.h, 16)
            eng.dma_start(s.x[0:rest, full, :], x[full * P:NODES, :]).then_inc(ld.h, 16)
            ld.at += 32
            eng.wait_ge(ld.h, ld.at)


def store_nodes(p, s, out):
    ld = p.sem("loaded")
    full, rest = BLK - 1, NODES - (BLK - 1) * P
    with p.block() as block:
        @block.sync
        def _(eng):
            eng.dma_start(out[0:full * P, :].rearrange("(b q) f -> q b f", q=P), s.x[:, 0:full, :]).then_inc(ld.h, 16)
            eng.dma_start(out[full * P:NODES, :], s.x[0:rest, full, :]).then_inc(ld.h, 16)
            ld.at += 32
            eng.wait_ge(ld.h, ld.at)


class Sorting:
    pass


def build(nc, ins, out, debug=None):
    ctx = ExitStack()
    with ctx:
        p = Program(nc, ctx, ins, out)
        s = Sorting()
        constants(p)
        s.key_rows = p.dram("key_rows", [RTILES * P * P], FP16)
        s.sblk_rows = p.dram("sblk_rows", [RTILES * P * P], FP16)
        s.type_rows = p.dram("type_rows", [RTILES * P * P], FP16)
        s.ends_d = p.dram("ends_d", [BLK * BLK], FP32)
        s.blocks_d = p.dram("blocks_d", [2, KT * P], FP32)
        s.sorted_d = p.dram("sorted_d", [P * CHUNKS + P, REC], FP32)
        first = ExitStack()
        with first:
            s.rec = p.sb("rec", [P, ROWS, 4], FP32, first)
            s.edge_cols = p.sb("edge_cols", [P, 3, ROWS], FP32, first)
            load_edges(p, s)
            s.before = p.sb("before", [BLK, ROWS + 1, BLK], FP32, first)
            s.ones_row = p.sb("ones_row", [BLK, ROWS], FP32, first)
            s.empty = p.sb("empty", [P, QUARTERS, REC], FP32, first)
            s.rel_parts = p.sb("rel_parts", [P, RB, 3, LAYERS * HEADS], BF16, first)
            pool = p.sem("pool")
            with p.block() as block:
                @block.gpsimd
                def _(eng):
                    eng.memset(s.ones_row[:], 1.0).then_inc(pool.h, 1)
                    eng.memset(s.empty[:], 0.0).then_inc(pool.h, 1)
                    eng.wait_ge(pool.h, pool.at + 2)
                    eng.memset(s.empty[:, :, 0:2], float(NONE)).then_inc(pool.h, 1)
                    pool.at += 3
            count_buckets(p, s)
            place_buckets(p, s)
            relation_scores(p, s)
            sort_edges(p, s)
        s.pos_rows = [p.dram(f"pos_rows{i}", [CHUNKS * P], FP16) for i in range(3)]
        s.e = p.sb("e", [P, CHUNKS, REC], FP32)
        s.ctl = p.sb("ctl", [P, (QUARTERS + 1) * CTL], I16)
        s.x = p.sb("x_now", [P, BLK, D], FP32)
        s.cat = p.sb("cat", [P, BLK, P], FP32)
        s.deg = p.sb("deg", [P, BLK], FP32)
        s.zeros = p.sb("zeros", [P, 512], BF16)
        s.regs = [nc.tensor.alloc_register(f"block_{i}") for i in range(16)]
        s.vregs = [nc.vector.alloc_register(f"vblock_{i}") for i in range(4)]
        load_sorted(p, s)
        load_nodes(p, s)
        for name, net in (("m", message_net), ("r", relation_net), ("s", sage_net), ("a", attention_net)):
            net(p, s)
            if debug == name:
                break
        store_nodes(p, s, out)


_INS = ['x', 'src', 'dst', 'edge_type_500', 'edge_type_8', 'edge_weight', 'L0_gnn_edge_W', 'L0_gnn_edge_b',
        'L0_gnn_node_W', 'L0_gnn_node_b', 'L1_gnn_W_enc', 'L1_gnn_b_enc', 'L1_gnn_W_rel', 'L1_gnn_W_self',
        'L1_gnn_bias', 'L2_gnn_W1l', 'L2_gnn_b1', 'L2_gnn_W1r', 'L2_gnn_W2l', 'L2_gnn_b2', 'L2_gnn_W2r',
        'L3_gnn_relation_embed', 'L3_gnn_ln_gamma', 'L3_gnn_ln_beta', 'L3_gnn_W_h', 'L3_gnn_W_t', 'L3_gnn_W_r',
        'L3_gnn_att_h', 'L3_gnn_att_t', 'L3_gnn_att_r', 'L3_gnn_W_o']


def kernel(**inputs):
    import numpy as _np
    import concourse.bacc as _bacc
    from concourse import mybir as _mybir
    from concourse.bass_utils import run_bass_kernel_spmd as _run

    nc = _bacc.Bacc("TRN2", target_bir_lowering=False, num_devices=1)
    arrays, ins = {}, {}
    for name in _INS:
        a = _np.ascontiguousarray(inputs[name])
        arrays[name] = a
        ins[name] = nc.dram_tensor(name, a.shape, _mybir.dt.from_np(a.dtype), kind="ExternalInput").ap()
    out = nc.dram_tensor("out", (NODES, D), FP32, kind="ExternalOutput").ap()
    build(nc, ins, out)
    r = _run(nc, [arrays], core_ids=[0])
    return r.results[0]["out"]
```
